# Optimizing a Trainium2 kernel written in Bass

```python
import numpy as np
import jax
import jax.numpy as jnp

def _softmax(x, axis=-1):
    return jax.nn.softmax(x, axis=axis)

def _gelu(x):
    return jax.nn.gelu(x, approximate=True)

def _silu(x):
    return jax.nn.silu(x)

def _sigmoid(x):
    return jax.nn.sigmoid(x)

def _layernorm(x, axis=-1, eps=1e-05):
    m = jnp.mean(x, axis=axis, keepdims=True)
    v = jnp.var(x, axis=axis, keepdims=True)
    return (x - m) / jnp.sqrt(v + eps)

def _scatter_add(tgt, idx, src, axis=0):
    return tgt.at[idx].add(src)

def _segment_sum(src, seg, n):
    return jax.ops.segment_sum(src, seg, n)
kernel_name = 'mk_flamingo_gated_d1_seqx_r4_0a3a29'

def setup_inputs(seed: int=0):
    np.random.seed(seed)
    _w = jnp.asarray

    def _rec_inputs():
        import jax
        import jax.numpy as jnp
        _rk = jax.random.key(seed)
        x = -0.0002928 + 1 * jax.random.normal(jax.random.fold_in(_rk, 1), (16, 256, 256), jnp.float32)
        _lenS = 256 - jax.random.randint(jax.random.fold_in(_rk, 7), (16,), 0, max(1, 256 // 4) + 1, jnp.int32)
        _lenS2 = 256 - jax.random.randint(jax.random.fold_in(_rk, 8), (16,), 0, max(1, 256 // 4) + 1, jnp.int32)
        _ctx_1024P = jax.random.normal(jax.random.fold_in(_rk, 11), (16, 16, 256), jnp.float32)
        _ctx_1024c = jax.random.dirichlet(jax.random.fold_in(_rk, 511), 0.3 * jnp.ones((16,), jnp.float32), (16, 256))
        _ctx_1024t = jnp.einsum('bsk,bkd->bsd', _ctx_1024c, _ctx_1024P)
        _ctx_1024t = _ctx_1024t * jax.lax.rsqrt(jnp.mean(jnp.square(_ctx_1024t)) + 1e-12) * 0.953939
        ctx_1024 = -1.39393e-06 + 0.999914 * (_ctx_1024t + 0.3 * jax.random.normal(jax.random.fold_in(_rk, 611), (16, 256, 256), jnp.float32))
        _g = jax.random.normal(jax.random.fold_in(_rk, 9001), (2, 1), jnp.float32)
        _g = jnp.sign(_g) * jnp.maximum(jnp.abs(_g), 1.0) + (_g == 0) * 1.0
        g_xattn = _g[0]
        g_ffn = _g[1]
        return (x, ctx_1024, g_xattn, g_ffn)
    x, ctx_1024, g_xattn, g_ffn = _rec_inputs()

    def _L0_xattn_setup():
        import math
        import jax, jax.numpy as jnp
        import numpy as np
        B, S, H, NH = (2, 512, 256, 4)
        DH = H // NH

        def _mlstm_parallel(qh, kh, vh, ig, fg, eps=1e-06):
            b, nh, s, dh = qh.shape
            log_f = jax.nn.log_sigmoid(fg)
            pcs = jnp.pad(jnp.cumsum(log_f, axis=-1), ((0, 0), (0, 0), (1, 0)))
            mat = pcs[..., :, None] - pcs[..., None, :]
            ltr = jnp.tril(jnp.ones((s, s), dtype=bool))
            log_fg_matrix = jnp.where(ltr, mat[..., 1:, 1:], -jnp.inf)
            log_D = log_fg_matrix + ig[..., None, :]
            max_log_D = jnp.max(log_D, axis=-1, keepdims=True)
            D = jnp.exp(log_D - max_log_D)
            qk = jnp.einsum('bhsd,bhtd->bhst', qh, kh) / math.sqrt(dh)
            C = qk * D
            normalizer = jnp.maximum(jnp.abs(C.sum(axis=-1, keepdims=True)), jnp.exp(-max_log_D))
            Cn = C / (normalizer + eps)
            return jnp.einsum('bhst,bhtd->bhsd', Cn, vh)
        key = jax.random.key(seed)
        ks = jax.random.split(key, 8)
        gate_std = 1.0 / math.sqrt(3 * H)
        return {'q': jax.random.normal(ks[0], (B, S, H), jnp.float32), 'k': jax.random.normal(ks[1], (B, S, H), jnp.float32), 'v': jax.random.normal(ks[2], (B, S, H), jnp.float32), 'w_igate': jax.random.normal(ks[3], (NH, 3 * H), jnp.float32) * gate_std, 'b_igate': jax.random.normal(ks[4], (NH,), jnp.float32) * 0.1, 'w_fgate': jax.random.normal(ks[5], (NH, 3 * H), jnp.float32) * gate_std, 'b_fgate': jnp.linspace(3.4, 6.0, NH, dtype=jnp.float32), 'ln_weight': jnp.zeros((H,), jnp.float32)}
    _L0_xattn_all = _L0_xattn_setup()
    _L0_xattn_in = {k: v for k, v in _L0_xattn_all.items() if k in ('w_igate', 'b_igate', 'w_fgate', 'b_fgate', 'ln_weight')}
    del _L0_xattn_all

    def _L0_ffn_setup():
        import jax, jax.numpy as jnp
        import numpy as np
        N_GROUP = 8
        TOPK_GROUP = 4
        TOPK = 8
        ROUTED_SCALE = 2.5
        B, S, D, F, E = (4, 512, 256, 128, 64)

        def _route(x, w_router, b_router):
            scores = jax.nn.sigmoid(jnp.einsum('bsd,de->bse', x, w_router)).astype(jnp.float32)
            swb = scores + b_router
            e = scores.shape[-1]
            group_scores = jnp.sum(jax.lax.top_k(swb.reshape(swb.shape[:-1] + (N_GROUP, -1)), 2)[0], axis=-1)
            group_idx = jax.lax.top_k(group_scores, TOPK_GROUP)[1]
            mask = jnp.any(jnp.arange(N_GROUP)[:, None] == group_idx[..., None, :], axis=-1)
            mask = jnp.repeat(mask, e // N_GROUP, axis=-1)
            masked_scores = jnp.where(mask, swb, 0.0)
            topk_idx = jax.lax.top_k(masked_scores, TOPK)[1]
            topk_w = jnp.take_along_axis(scores, topk_idx, axis=-1).astype(jnp.float32)
            topk_w = ROUTED_SCALE * topk_w / (jnp.sum(topk_w, axis=-1)[..., None] + 1e-20)
            return (topk_w, topk_idx)

        def _moe_forward(x, w_router, b_router, we_gate, we_up, we_down, ws_gate, ws_up, ws_down):
            b, s, d = x.shape
            e = we_gate.shape[0]
            topk_w, topk_idx = _route(x, w_router, b_router)
            x_flat = x.reshape(-1, d)
            idx_flat = topk_idx.reshape(-1)
            sort = jnp.argsort(idx_flat)
            tok = sort // TOPK
            x_sorted = x_flat[tok]
            group_sizes = jnp.bincount(idx_flat, length=e).astype(jnp.int32)
            g = jax.lax.ragged_dot(x_sorted, we_gate, group_sizes)
            u = jax.lax.ragged_dot(x_sorted, we_up, group_sizes)
            o = jax.lax.ragged_dot(jax.nn.silu(g) * u, we_down, group_sizes)
            w_sorted = topk_w.reshape(-1)[sort].astype(o.dtype)
            y = jnp.zeros_like(x_flat).at[tok].add(o * w_sorted[:, None])
            y = y.reshape(b, s, d)
            shared = jnp.einsum('btf,fd->btd', jax.nn.silu(jnp.einsum('btd,df->btf', x, ws_gate)) * jnp.einsum('btd,df->btf', x, ws_up), ws_down)
            return y + shared
        key = jax.random.key(seed)
        ks = jax.random.split(key, 10)
        sd = 1.0 / np.sqrt(D)
        sf = 1.0 / np.sqrt(F)
        return {'x': jax.random.normal(ks[0], (B, S, D), jnp.float32), 'w_router': jax.random.normal(ks[1], (D, E), jnp.float32) * sd, 'b_router': jax.random.normal(ks[2], (E,), jnp.float32) * 0.1, 'we_gate': jax.random.normal(ks[3], (E, D, F), jnp.float32) * sd, 'we_up': jax.random.normal(ks[4], (E, D, F), jnp.float32) * sd, 'we_down': jax.random.normal(ks[5], (E, F, D), jnp.float32) * sf, 'ws_gate': jax.random.normal(ks[6], (D, F), jnp.float32) * sd, 'ws_up': jax.random.normal(ks[7], (D, F), jnp.float32) * sd, 'ws_down': jax.random.normal(ks[8], (F, D), jnp.float32) * sf}
    _L0_ffn_all = _L0_ffn_setup()
    _L0_ffn_in = {k: v for k, v in _L0_ffn_all.items() if k in ('w_router', 'b_router', 'we_gate', 'we_up', 'we_down', 'ws_gate', 'ws_up', 'ws_down')}
    del _L0_ffn_all
    return {'x': x, 'ctx_1024': ctx_1024, 'g_xattn': g_xattn, 'g_ffn': g_ffn, 'L0_xattn_w_igate': _L0_xattn_in['w_igate'], 'L0_xattn_b_igate': _L0_xattn_in['b_igate'], 'L0_xattn_w_fgate': _L0_xattn_in['w_fgate'], 'L0_xattn_b_fgate': _L0_xattn_in['b_fgate'], 'L0_xattn_ln_weight': _L0_xattn_in['ln_weight'], 'L0_ffn_w_router': _L0_ffn_in['w_router'], 'L0_ffn_b_router': _L0_ffn_in['b_router'], 'L0_ffn_we_gate': _L0_ffn_in['we_gate'], 'L0_ffn_we_up': _L0_ffn_in['we_up'], 'L0_ffn_we_down': _L0_ffn_in['we_down'], 'L0_ffn_ws_gate': _L0_ffn_in['ws_gate'], 'L0_ffn_ws_up': _L0_ffn_in['ws_up'], 'L0_ffn_ws_down': _L0_ffn_in['ws_down']}

def reference(x, ctx_1024, g_xattn, g_ffn, L0_xattn_w_igate, L0_xattn_b_igate, L0_xattn_w_fgate, L0_xattn_b_fgate, L0_xattn_ln_weight, L0_ffn_w_router, L0_ffn_b_router, L0_ffn_we_gate, L0_ffn_we_up, L0_ffn_we_down, L0_ffn_ws_gate, L0_ffn_ws_up, L0_ffn_ws_down):
    import jax
    import jax.numpy as jnp

    def _L0_xattn_ref(q, k, v, w_igate, b_igate, w_fgate, b_fgate, ln_weight):
        import math
        import jax, jax.numpy as jnp
        import numpy as np
        B, S, H, NH = (2, 512, 256, 4)
        DH = H // NH

        def _mlstm_parallel(qh, kh, vh, ig, fg, eps=1e-06):
            b, nh, s, dh = qh.shape
            log_f = jax.nn.log_sigmoid(fg)
            pcs = jnp.pad(jnp.cumsum(log_f, axis=-1), ((0, 0), (0, 0), (1, 0)))
            mat = pcs[..., :, None] - pcs[..., None, :]
            ltr = jnp.tril(jnp.ones((s, s), dtype=bool))
            log_fg_matrix = jnp.where(ltr, mat[..., 1:, 1:], -jnp.inf)
            log_D = log_fg_matrix + ig[..., None, :]
            max_log_D = jnp.max(log_D, axis=-1, keepdims=True)
            D = jnp.exp(log_D - max_log_D)
            qk = jnp.einsum('bhsd,bhtd->bhst', qh, kh) / math.sqrt(dh)
            C = qk * D
            normalizer = jnp.maximum(jnp.abs(C.sum(axis=-1, keepdims=True)), jnp.exp(-max_log_D))
            Cn = C / (normalizer + eps)
            return jnp.einsum('bhst,bhtd->bhsd', Cn, vh)
        b, s, h = q.shape
        nh = b_igate.shape[0]
        dh = h // nh
        gin = jnp.concatenate([q, k, v], axis=-1)
        ig = jnp.einsum('bsd,hd->bhs', gin, w_igate) + b_igate[None, :, None]
        fg = jnp.einsum('bsd,hd->bhs', gin, w_fgate) + b_fgate[None, :, None]
        qh = q.reshape(b, s, nh, dh).transpose(0, 2, 1, 3)
        kh = k.reshape(b, s, nh, dh).transpose(0, 2, 1, 3)
        vh = v.reshape(b, s, nh, dh).transpose(0, 2, 1, 3)
        hst = _mlstm_parallel(qh, kh, vh, ig, fg)
        mean = hst.mean(axis=-1, keepdims=True)
        var = hst.var(axis=-1, keepdims=True)
        hn = (hst - mean) / jnp.sqrt(var + 1e-05)
        scale = (1.0 + ln_weight).reshape(nh, dh)
        hn = hn * scale[None, :, None, :]
        return hn.transpose(0, 2, 1, 3).reshape(b, s, h)

    def _L0_ffn_ref(x, w_router, b_router, we_gate, we_up, we_down, ws_gate, ws_up, ws_down):
        import jax, jax.numpy as jnp
        import numpy as np
        N_GROUP = 8
        TOPK_GROUP = 4
        TOPK = 8
        ROUTED_SCALE = 2.5
        B, S, D, F, E = (4, 512, 256, 128, 64)

        def _route(x, w_router, b_router):
            scores = jax.nn.sigmoid(jnp.einsum('bsd,de->bse', x, w_router)).astype(jnp.float32)
            swb = scores + b_router
            e = scores.shape[-1]
            group_scores = jnp.sum(jax.lax.top_k(swb.reshape(swb.shape[:-1] + (N_GROUP, -1)), 2)[0], axis=-1)
            group_idx = jax.lax.top_k(group_scores, TOPK_GROUP)[1]
            mask = jnp.any(jnp.arange(N_GROUP)[:, None] == group_idx[..., None, :], axis=-1)
            mask = jnp.repeat(mask, e // N_GROUP, axis=-1)
            masked_scores = jnp.where(mask, swb, 0.0)
            topk_idx = jax.lax.top_k(masked_scores, TOPK)[1]
            topk_w = jnp.take_along_axis(scores, topk_idx, axis=-1).astype(jnp.float32)
            topk_w = ROUTED_SCALE * topk_w / (jnp.sum(topk_w, axis=-1)[..., None] + 1e-20)
            return (topk_w, topk_idx)

        def _moe_forward(x, w_router, b_router, we_gate, we_up, we_down, ws_gate, ws_up, ws_down):
            b, s, d = x.shape
            e = we_gate.shape[0]
            topk_w, topk_idx = _route(x, w_router, b_router)
            x_flat = x.reshape(-1, d)
            idx_flat = topk_idx.reshape(-1)
            sort = jnp.argsort(idx_flat)
            tok = sort // TOPK
            x_sorted = x_flat[tok]
            group_sizes = jnp.bincount(idx_flat, length=e).astype(jnp.int32)
            g = jax.lax.ragged_dot(x_sorted, we_gate, group_sizes)
            u = jax.lax.ragged_dot(x_sorted, we_up, group_sizes)
            o = jax.lax.ragged_dot(jax.nn.silu(g) * u, we_down, group_sizes)
            w_sorted = topk_w.reshape(-1)[sort].astype(o.dtype)
            y = jnp.zeros_like(x_flat).at[tok].add(o * w_sorted[:, None])
            y = y.reshape(b, s, d)
            shared = jnp.einsum('btf,fd->btd', jax.nn.silu(jnp.einsum('btd,df->btf', x, ws_gate)) * jnp.einsum('btd,df->btf', x, ws_up), ws_down)
            return y + shared
        return _moe_forward(x, w_router, b_router, we_gate, we_up, we_down, ws_gate, ws_up, ws_down)
    x = x + jnp.tanh(g_xattn[0]) * _L0_xattn_ref(_layernorm(x, axis=-1), ctx_1024, ctx_1024, L0_xattn_w_igate, L0_xattn_b_igate, L0_xattn_w_fgate, L0_xattn_b_fgate, L0_xattn_ln_weight)
    x = x + jnp.tanh(g_ffn[0]) * _L0_ffn_ref(_layernorm(x, axis=-1), L0_ffn_w_router, L0_ffn_b_router, L0_ffn_we_gate, L0_ffn_we_up, L0_ffn_we_down, L0_ffn_ws_gate, L0_ffn_ws_up, L0_ffn_ws_down)
    return x

_drawn_inputs = setup_inputs


def setup_inputs(seed=0):
    import zlib

    import numpy as np

    out = dict(_drawn_inputs(seed))
    spreads = {'L0_xattn_ln_weight': (0.0, 0.1)}
    factors = {'L0_xattn_b_igate': 64.0}
    for name, (base, spread) in spreads.items():
        noise = np.random.default_rng([zlib.crc32(name.encode()), seed]).standard_normal(out[name].shape)
        drawn = base * np.exp(spread * noise) if base else spread * noise
        out[name] = jnp.asarray(drawn.astype(out[name].dtype))
    for name, factor in factors.items():
        out[name] = (out[name] * factor).astype(out[name].dtype)
    return out
```

```python
import concourse.bass as bass
from concourse import mybir
from contextlib import ExitStack


class Steps:

    def __init__(self, sem, per_pass):
        self.sem, self.per_pass, self.n, self.turn = sem, per_pass, 0, 0

    def begin(self, turn):
        self.n, self.turn = 0, turn

    def end(self):
        assert self.n == self.per_pass, self.n

    def did(self, instruction):
        instruction.then_inc(self.sem, 1)
        self.n += 1
        return self.n

    def wait(self, engine, step):
        engine.wait_ge(self.sem, self.turn * self.per_pass + step)


def reached(engine, sem, value):
    if not (isinstance(value, int) and value <= 0):
        engine.wait_ge(sem, value)


def flamingo_moe(nc, x, ctx, g_xattn, g_ffn, w_gates, b_gates, ln_weight, w_router, b_router,
                 we, ws_gate, ws_up, ws_down, out):
    fp32, f32r, bf16, i32 = (mybir.dt.float32, mybir.dt.float32r, mybir.dt.bfloat16, mybir.dt.int32)
    ALU = mybir.AluOpType
    ACT = mybir.ActivationFunctionType
    AX = mybir.AxisListType

    B, S, D = x.shape
    P = 128
    U = S // P
    KC = D // P
    NH = 4
    DH = D // NH
    E = w_router.shape[1]
    F = ws_gate.shape[1]
    NG, GS, TOPG, K = 8, E // 8, 4, 8
    N = B * S
    NT = N // P
    REG = N
    TILES = -(-(N * K + E * (P - 1)) // P // 8) * 8
    TC = -(-TILES // P)
    WE = 3 * D
    RW, RX, RO = 8, 8, 4
    NB = B // 2
    EPS_LN, BIG = 1e-5, 3.0e38
    EXP_AND_LN = 6

    ex = ExitStack()
    with ex:
        def sb(name, shape, dt=fp32):
            return ex.enter_context(nc.sbuf_tensor(name, shape, dt))

        def sem(name):
            return ex.enter_context(nc.semaphore(name))

        xs = nc.dram_tensor("expert_rows", (E * REG, D), fp32, kind="Internal").ap()
        os_ = nc.dram_tensor("expert_out", (TILES * P, D), fp32, kind="Internal").ap()

        ident = sb("ident", [P, P])
        identb = sb("identb", [P, P], bf16)
        tri_inc = sb("tri_inc", [P, P])
        tri_exc = sb("tri_exc", [P, P], bf16)
        ones = sb("ones", [P, P])
        onesb = sb("onesb", [P, P], bf16)
        mask = sb("mask", [P, P], bf16)
        head_row = sb("head_row", [NH, NH, P])
        zeros4 = sb("zeros4", [NH, S])
        earlier = sb("earlier", [P, NG, NG])
        later = sb("later", [P, NG, NG])
        wg = sb("wg", [P, 3 * KC, 2 * NH])
        wctx = sb("wctx", [P, KC, 2 * NH])
        gbias = sb("gbias", [P, 2 * NH])
        lnw = sb("lnw", [P, D])
        wt = sb("wt", [P, D])
        gate_in = sb("gate_in", [P, 2])
        gate_t = sb("gate_t", [P, 2])
        wr = sb("wr", [P, KC, E])
        rbias = sb("rbias", [P, E])
        wsg = sb("wsg", [P, KC, F])
        wsu = sb("wsu", [P, KC, F])
        wsd = sb("wsd", [P, D])
        x2 = sb("x2", [P, NT, D])
        ysh = sb("ysh", [P, NT, D])
        placeall = sb("placeall", [P, B, U * K])
        wkall = sb("wkall", [P, B, U * K])
        place = sb("place", [P, E])
        place0 = sb("place0", [P, E])
        rows = [sb(f"rows{q}", [P, U, D]) for q in range(2)]
        x2now = [sb(f"x2now{q}", [P, U, D]) for q in range(2)]
        idx = [sb(f"idx{q}", [P, U * K], i32) for q in range(2)]
        cnt, cntf, cum, qoff, junk = (sb(n, [P, E]) for n in ("cnt", "cntf", "cum", "qoff", "junk"))
        cnti, cnts = sb("cnti", [P, E], i32), sb("cnts", [P, E], i32)
        tno, tsub, eid, aoff, last, eidf = (sb(n, [P, TC]) for n in (
            "tno", "tsub", "eid", "aoff", "last", "eidf"))
        eidi, eids = sb("eidi", [P, TC], i32), sb("eids", [P, TC], i32)
        padrow, legit, legrow, toolow, padsel = (sb(n, [P, E]) for n in ("padrow", "legit", "legrow", "toolow", "padsel"))
        anyrow = sb("anyrow", [P, 1])
        move = sb("move", [P, E])
        moves = sb("moves", [P, K, E])
        moved = [sb(f"moved{q}", [P, K]) for q in range(2)]
        NQ = 3
        RING, NEED, XROW = range(NQ)
        tcol = sb("tcol", [P, NQ, TC])
        tab = sb("tab", [1, NQ * TC * P], i32)
        tab_pad = sb("tab_pad", [1, E], i32)
        tab_end = sb("tab_end", [1, E], i32)
        zrow = sb("zrow", [P, D])

        ex1 = ExitStack()

        def sb1(name, shape, dt=fp32):
            return ex1.enter_context(nc.sbuf_tensor(name, shape, dt))

        xin = [sb1(f"xin{q}", [P, U, D]) for q in range(2)]
        cin = [sb1(f"cin{q}", [P, U, D]) for q in range(2)]
        xn = sb1("xn", [P, U, D])
        xnT = [sb1(f"xnT{q}", [P, KC, S]) for q in range(2)]
        ctxT = [sb1(f"ctxT{q}", [P, KC, S]) for q in range(2)]
        vext = [sb1(f"vext{q}", [P, U, NH, DH + 1]) for q in range(2)]
        st1, mv1, ve1, ln1, r1, t1, rstd1 = (sb1(n, s) for n, s in (
            ("st1", [P, U, 6]), ("mv1", [P, U, 2]), ("ve1", [P, U]), ("ln1", [P, U]), ("r1", [P, U]),
            ("t1", [P, U]), ("rstd1", [P, U])))
        gate = sb1("gate", [P, U, 2 * NH])
        absf, expf, sp, lf, ng, cfs, nmd = (sb1(n, [P, U, NH]) for n in
                                            ("absf", "expf", "sp", "lf", "ng", "cfs", "nmd"))
        gcol = [sb1(f"gcol{q}", [P, U, NH]) for q in range(2)]
        negm = [sb1(f"negm{q}", [NH, S]) for q in range(2)]
        enm = [sb1(f"enm{q}", [P, U, NH]) for q in range(2)]
        decay = [sb1(f"decay{q}", [P, S + P]) for q in range(2)]
        cmat = [sb1(f"cmat{q}", [P, S + P]) for q in range(2)]
        den, floor_, deneps, rden = (sb1(n, [P, U, NH]) for n in ("den", "floor", "deneps", "rden"))
        hst = sb1("hst", [P, U * NH, DH])
        hc = sb1("hc", [P, U * NH, DH])
        hn = sb1("hn", [P, U * NH, DH])
        hw = sb1("hw", [P, U * NH, DH])
        st2 = sb1("st2", [P, U * NH, 6])
        sm2, dm2, q2, m2, v2, ve2, mean2, ln2, r2, t2, rstd2 = (sb1(n, [P, U * NH]) for n in (
            "sm2", "dm2", "q2", "m2", "v2", "ve2", "mean2", "ln2", "r2", "t2", "rstd2"))
        st3, mv3, ve3, ln3, r3, t3, rstd3 = (sb1(n, s) for n, s in (
            ("st3", [P, U, 6]), ("mv3", [P, U, 2]), ("ve3", [P, U]), ("ln3", [P, U]), ("r3", [P, U]),
            ("t3", [P, U]), ("rstd3", [P, U])))
        x2T = sb1("x2T", [P, KC, S])
        es, es1, score, biased, masked, repl, wsel, wn, pos, posm = (sb1(n, [P, U, E]) for n in (
            "es", "es1", "score", "biased", "masked", "repl", "wsel", "wn", "pos", "posm"))
        chosen = sb1("chosen", [P, U, E], bf16)
        top_in_group = sb1("top_in_group", [P, U * NG, 8])
        gscore = sb1("gscore", [P, U, NG])
        gge, ggt, grank3 = (sb1(n, [P, U, NG, NG]) for n in ("gge", "ggt", "grank3"))
        grank, gmask = (sb1(n, [P, U, NG]) for n in ("grank", "gmask"))
        top = sb1("top", [P, U, 8])
        wsum, wsume, wrec = (sb1(n, [P, U]) for n in ("wsum", "wsume", "wrec"))
        place8 = sb1("place8", [P, U, 8])
        picked = sb1("picked", [P, U * K, E])
        eg, eg1, sg, hg, hs = (sb1(n, [P, S]) for n in ("eg", "eg1", "sg", "hg", "hs"))
        ex1.close()

        psum = ex.enter_context(nc.psum_tensor("psum", [P, 8, 512], fp32))
        bS = [psum[:, 0, :], psum[:, 1, :]]
        bM = psum[:, 2, :]
        bAV = [psum[:, 3, :], psum[:, 4, :]]
        bT = psum[:, 5, :]
        bB0 = psum[:, 6, :]
        bB1 = psum[:, 7, :]

        s_const, s_constv, s_small, s_ready0 = map(sem, ("const_made", "const_dve", "small_loaded", "const_ready"))
        s_tanh = sem("gates_tanh")
        x_loaded = [sem(f"x_loaded{q}") for q in range(2)]
        c_loaded = [sem(f"ctx_loaded{q}") for q in range(2)]
        (var1_ready, guess1_ready, xn_ready, ctx_transposed, ctxT_ready, vext_ready, xn_transposed,
         xnT_ready, gates_ready, absf_ready, softplus_ready, logf_ready, cumf_ready, ng_ready,
         gcol_ready, ngT_ready, negm_ready, negm_cols_ready, nmd_ready, enm_ready) = map(sem, (
            "var1_ready", "guess1_ready", "xn_ready", "ctx_transposed", "ctxT_ready", "vext_ready",
            "xn_transposed", "xnT_ready", "gates_ready", "absf_ready", "softplus_ready", "logf_ready",
            "cumf_ready", "ng_ready", "gcol_ready", "ngT_ready", "negm_ready", "negm_cols_ready",
            "nmd_ready", "enm_ready"))
        scores_ready, decay_arg_ready, decay_ready, cmat_ready, av_done = map(sem, (
            "scores_ready", "decay_arg_ready", "decay_ready", "cmat_ready", "av_done"))
        (hst_done, var2_ready, guess2_ready, x2_ready, x2_kept, var3_ready, guess3_ready, row_ready,
         x2_transposed, x2T_ready, logits_ready, es_ready, chosen_ready, ranks_ready, place_done,
         idx_ready, gu_ready, eg_ready, hs_ready, y_ready, ysh_done) = map(sem, (
            "hst_done", "var2_ready", "guess2_ready", "x2_ready", "x2_kept", "var3_ready", "guess3_ready",
            "row_ready", "x2_transposed", "x2T_ready", "logits_ready", "es_ready", "chosen_ready",
            "ranks_ready", "place_done", "idx_ready", "gu_ready", "eg_ready",
            "hs_ready", "y_ready", "ysh_done"))
        scattered = [sem(f"scattered{q}") for q in range(2)]
        pool_mark, dve_mark = sem("pool_mark"), sem("dve_mark")
        dveG = Steps(sem("dve_gates_step"), 9)
        dveH = Steps(sem("dve_heads_step"), 27)
        dveL = Steps(sem("dve_route_step"), 69)
        actG = Steps(sem("act_gates_step"), 2)
        actH = Steps(sem("act_heads_step"), 1)
        actL = Steps(sem("act_route_step"), 1)
        dveT = Steps(sem("dve_table_step"), 100)
        tcol_ready, tab_rows, tab_ready, pads_done = map(sem, ("tcol_ready", "tab_rows", "tab_ready", "pads_done"))

        xt = [sb(f"xt{q}", [P, D]) for q in range(RX)]
        raw = [sb(f"raw{q}", [P, WE]) for q in range(2)]
        wsp = sb("wsp", [P, 2, RW * WE], f32r)
        whi, wlo = wsp[:, 0, :], wsp[:, 1, :]
        xhi = [sb(f"xhi{q}", [P, D], f32r) for q in range(4)]
        xlo = [sb(f"xlo{q}", [P, D], f32r) for q in range(4)]
        sgt = [sb(f"sgt{q}", [P, F]) for q in range(2)]
        ht = [sb(f"ht{q}", [P, F]) for q in range(2)]
        hhi = [sb(f"hhi{q}", [P, P], f32r) for q in range(2)]
        hlo = [sb(f"hlo{q}", [P, P], f32r) for q in range(2)]
        ot = [sb(f"ot{q}", [P, D]) for q in range(RO)]
        idxs = [sb(f"idxs{q}", [P, K], i32) for q in range(2)]
        got = [sb(f"got{q}", [P, K, D]) for q in range(2)]
        wk = [sb(f"wk{q}", [P, K]) for q in range(2)]
        pk = [sb(f"pk{q}", [P, K]) for q in range(2)]
        acc = sb("acc", [P, 2, D])
        res = [sb(f"res{q}", [P, D]) for q in range(2)]

        bX = [psum[:, 0, 0:D], psum[:, 1, 0:D]]
        bG = [psum[:, 2, 0:2 * F], psum[:, 3, 0:2 * F]]
        bH = [psum[:, 4, 0:P], psum[:, 5, 0:P]]
        bO = [psum[:, 6, 0:D], psum[:, 7, 0:D]]

        rows_loaded = [sem(f"rows_loaded{q}") for q in range(RX)]
        raw_loaded = [sem(f"raw_loaded{q}") for q in range(2)]
        weights_hi, weights_ready, xT_ready, xhi_ready, xlo_ready, gu2_ready, silu_ready, h_ready, hT_ready, hhi_ready, \
            hlo_ready, o_ready, ot_ready = map(sem, (
                "weights_hi", "weights_ready", "tile_xT_ready", "tile_xhi_ready", "tile_xlo_ready", "tile_gu_ready",
                "tile_silu_ready", "tile_h_ready", "tile_hT_ready", "tile_hhi_ready", "tile_hlo_ready",
                "tile_o_ready", "tile_ot_ready"))
        stored = [sem(f"tile_stored{q}") for q in range(RO)]
        idxs_ready, wk_ready, ends_zeroed = map(sem, ("combine_index_ready", "combine_weights_ready", "ends_zeroed"))
        gathered = [sem(f"gathered{q}") for q in range(2)]
        dveI = Steps(sem("dve_index_step"), 9)
        dveC = Steps(sem("dve_combine_step"), 8)
        res_ready = sem("result_ready")
        res_stored = [sem(f"result_stored{q}") for q in range(2)]

        def entry(engine, what, s, low, high):
            return engine.value_load(tab[0:1, bass.ds(s + what * TC * P, 1)], min_val=low, max_val=high)

        def tiles(engine, step, lead=0, lag=0):
            for t in range(-lead, 8):
                step(t, t % 8)
            with engine.Fori(1, TILES // 8 - 1) as i:
                for q in range(8):
                    step(8 * i + q, q)
            for t in range(TILES - 8, TILES + lag):
                step(t, t % 8)

        def real(t):
            return not isinstance(t, int) or 0 <= t < TILES

        def phase2_sp(sp):
            sp.wait_ge(tab_ready, 3)
            sp.wait_ge(pads_done, 16 * E)
            for q in range(2):
                sp.wait_ge(scattered[q], U * K * 16 * NB)

            def step(t, q):
                a = t + 5
                if real(a):
                    qa = (q + 5) % RX
                    r = entry(sp, XROW, a, 0, E * REG - P)
                    reached(sp, xT_ready, a - RX + 1)
                    sp.dma_start(xt[qa][:], xs[bass.ds(r, P), :]).then_inc(rows_loaded[qa], 16)
                if real(t - 1):
                    reached(sp, ot_ready, t)
                    qo = (q - 1) % RO
                    sp.dma_start(os_[bass.ds((t - 1) * P, P), :], ot[qo][:]).then_inc(stored[qo], 16)

            tiles(sp, step, lead=5, lag=1)
            ov = out.rearrange("b (u p) d -> (b u) p d", p=P)

            def store(j, q):
                sp.wait_ge(res_ready, j + 1)
                sp.dma_start(ov[bass.ds(j, 1)].rearrange("a p d -> p (a d)"), res[q][:]).then_inc(res_stored[q], 16)

            with sp.Fori(0, NT // 2) as i:
                for q in range(2):
                    store(2 * i + q, q)
            for q in range(2):
                sp.wait_ge(res_stored[q], 16 * NT // 2)

        def phase2_pool(pool):
            pool.wait_ge(tab_ready, 3)

            def expert(e, q, n8):
                if not (isinstance(e, int) and e < 2):
                    pool.wait_ge(weights_ready, e - 1)
                    nc.gpsimd.sem_inc(pool_mark, 1)
                nc.gpsimd.dma_start(raw[q % 2][:], we[bass.ds(e, 1)].rearrange("a p n -> p (a n)")).then_inc(raw_loaded[q % 2], 16)

            def split(e, q, i):
                if not (isinstance(e, int) and e < RW):
                    end = pool.value_load(tab_end[0:1, bass.ds(e - RW, 1)], min_val=0, max_val=TILES)
                    pool.wait_ge(o_ready, end + 1)
                    nc.gpsimd.sem_inc(pool_mark, 1)
                pool.wait_ge(raw_loaded[q % 2], 16 * ((4 * i) + q // 2 + 1))
                nc.gpsimd.sem_inc(pool_mark, 1)
                w = slice(q * WE, (q + 1) * WE)
                nc.gpsimd.tensor_copy(whi[:, w], raw[q % 2][:]).then_inc(weights_hi, 1)
                pool.wait_ge(weights_hi, e + 1)
                nc.gpsimd.tensor_tensor(wlo[:, w], raw[q % 2][:], whi[:, w].bitcast(fp32), ALU.subtract).then_inc(weights_ready, 1)

            expert(0, 0, 0)
            for e in range(RW):
                expert(e + 1, (e + 1) % RW, 0)
                split(e, e, 0)
            with pool.Fori(1, E // RW - 1) as i:
                for q in range(RW):
                    expert(RW * i + q + 1, (q + 1) % RW, i)
                    split(RW * i + q, q, i)
            for e in range(E - RW, E):
                if e + 1 < E:
                    expert(e + 1, (e + 1) % RW, 0)
                split(e, e % RW, E // RW - 1)

            for q in range(RO):
                pool.wait_ge(stored[q], 16 * TILES // RO)

            def gather(j, q):
                pool.wait_ge(idxs_ready, j + 1)
                nc.gpsimd.sem_inc(pool_mark, 1)
                for k in range(K):
                    nc.gpsimd.indirect_dma_start(
                        out=got[q][:, k, :], out_offset=None, in_=os_,
                        in_offset=bass.IndirectOffsetOnAxis(ap=idxs[q][:, k:k + 1], axis=0)).then_inc(gathered[q], 16)

            with pool.Fori(0, NT // 2) as i:
                for q in range(2):
                    gather(2 * i + q, q)

        def phase2_pe(pe):
            mm, tr = nc.tensor.matmul, nc.tensor.transpose
            pe.wait_ge(tcol_ready, 1)
            for w in range(NQ):
                for c in range(TC):
                    j = w * TC + c
                    last = mm(psum[0:1, j // 4, (j % 4) * P:(j % 4 + 1) * P], tcol[:, w, c:c + 1], ident[:],
                              start=True, stop=True)
            last.then_inc(tab_rows, 1)
            pe.wait_ge(tab_ready, 3)
            pe.wait_ge(ysh_done, B)
            nc.tensor.sem_inc(o_ready, 1)

            def x_t(t, q):
                pe.wait_ge(rows_loaded[q], 16 * ((t - q) // 8 + 1) if isinstance(t, int) else 2 * (t - q) + 16)
                reached(pe, xlo_ready, t - 1)
                for k in range(KC):
                    last = tr(bX[q % 2][:, k * P:(k + 1) * P], xt[q][:, k * P:(k + 1) * P], ident[:])
                last.then_inc(xT_ready, 1)

            def up(t, q):
                need = entry(pe, NEED, t, 1, E)
                off = entry(pe, RING, t, 0, (RW - 1) * WE)
                pe.wait_ge(weights_ready, need)
                pe.wait_ge(xhi_ready, t + 1)
                pe.wait_ge(xlo_ready, t + 1)
                reached(pe, h_ready, t - 1)
                n = 0
                for xa, wa in ((xhi, whi), (xhi, wlo), (xlo, whi)):
                    for k in range(KC):
                        last = mm(bG[q % 2], xa[q % 4][:, k * P:(k + 1) * P], wa[:, bass.ds(off + k * 2 * F, 2 * F)],
                                  start=n == 0, stop=n == 5)
                        n += 1
                last.then_inc(gu2_ready, 1)

            def h_t(t, q):
                pe.wait_ge(h_ready, t + 1)
                reached(pe, hlo_ready, t - 1)
                tr(bH[q % 2], ht[q % 2][:], ident[:]).then_inc(hT_ready, 1)

            def down(t, q):
                off = entry(pe, RING, t, 0, (RW - 1) * WE)
                pe.wait_ge(hhi_ready, t + 1)
                pe.wait_ge(hlo_ready, t + 1)
                reached(pe, ot_ready, t - 1)
                for n, (ha, wa) in enumerate(((hhi, whi), (hhi, wlo), (hlo, whi))):
                    last = mm(bO[q % 2], ha[q % 2][:], wa[:, bass.ds(off + KC * 2 * F, D)], start=n == 0, stop=n == 2)
                last.then_inc(o_ready, 1)

            def step(t, q):
                if real(t + 1): up(t + 1, (q + 1) % 8)
                if real(t): h_t(t, q)
                if real(t + 3): x_t(t + 3, (q + 3) % 8)
                if real(t - 1): down(t - 1, (q - 1) % 8)

            tiles(pe, step, lead=3, lag=1)

        def phase2_act(act):
            A = nc.scalar.activation
            act.wait_ge(tab_ready, 3)
            with act.Fori(0, E) as e:
                r = act.value_load(tab_pad[0:1, bass.ds(e, 1)], min_val=0, max_val=E * REG - P)
                act.dma_start(xs[bass.ds(r, P), :], zrow[:]).then_inc(pads_done, 16)

            def step(t, q):
                a = t + 3
                if real(a):
                    qa = (q + 3) % 4
                    act.wait_ge(xT_ready, a + 1)
                    reached(act, gu2_ready, a - 3)
                    A(xhi[qa][:], bX[(q + 3) % 2], ACT.Copy).then_inc(xhi_ready, 1)
                a = t + 1
                if real(a):
                    act.wait_ge(gu2_ready, a + 1)
                    reached(act, h_ready, a - 1)
                    A(sgt[(q + 1) % 2][:], bG[(q + 1) % 2][:, 0:F], ACT.Silu).then_inc(silu_ready, 1)
                a = t - 1
                if real(a):
                    act.wait_ge(o_ready, a + 2)
                    n4 = (a - (q - 1) % 4) // 4 if isinstance(a, int) else None
                    if not isinstance(a, int):
                        act.wait_ge(stored[(q - 1) % 4], 4 * (a - (q - 1) % 4))
                    elif n4:
                        act.wait_ge(stored[(q - 1) % 4], 16 * n4)
                    A(ot[(q - 1) % 4][:], bO[(q - 1) % 2], ACT.Copy).then_inc(ot_ready, 1)

            tiles(act, step, lead=3, lag=1)

        def phase2_dve(dve):
            V = nc.vector
            T = dveT
            T.begin(0)

            def did(ins):
                T.wait(dve, T.did(ins))

            did(V.tensor_tensor(cnt[:], place[:], place0[:], ALU.subtract))
            did(V.tensor_scalar(cnti[:], cnt[:], float(P - 1), None, ALU.add))
            did(V.tensor_scalar(cnts[:], cnti[:], P.bit_length() - 1, None, ALU.arith_shift_right))
            did(V.tensor_copy(cntf[:], cnts[:]))
            did(V.memset(junk[:], 0.0))
            did(V.tensor_tensor_scan(cum[:], cntf[:], junk[:], 0.0, ALU.add, ALU.add))
            did(V.tensor_scalar(qoff[:], cntf[:], -float(P), float(REG), ALU.mult, ALU.add))
            did(V.tensor_scalar(last[:], cum[:, E - 1:E].to_broadcast([P, TC]), -1.0, None, ALU.add))
            did(V.tensor_tensor(tsub[:], tno[:], last[:], ALU.min))
            for c in range(TC):
                did(V.tensor_scalar(junk[:], cum[:], tsub[:, c:c + 1], 0.0, ALU.is_le, ALU.add, accum_out=eid[:, c:c + 1]))
                did(V.scalar_tensor_tensor(junk[:], cum[:], tsub[:, c:c + 1], qoff[:], ALU.is_le, ALU.mult,
                                           accum_out=aoff[:, c:c + 1]))
            did(V.scalar_tensor_tensor(tcol[:, XROW, :], tsub[:], float(P), aoff[:], ALU.mult, ALU.add))
            did(V.memset(move[:], 0.0))
            did(V.tensor_scalar(move[:, 1:E], qoff[:, 0:E - 1], -1.0, None, ALU.mult))
            did(V.tensor_scalar(tcol[:, NEED, :], eid[:], 1.0, None, ALU.add))
            did(V.tensor_scalar(padrow[:], place[:], -1.0, None, ALU.add))
            did(V.tensor_scalar(legit[:], cnt[:], float(REG - P), None, ALU.is_le))
            did(V.tensor_tensor(legrow[:], padrow[:], legit[:], ALU.mult))
            did(V.tensor_reduce(anyrow[:], legrow[:], AX.X, ALU.max))
            did(V.tensor_scalar(toolow[:], cnt[:], float(REG - P), None, ALU.is_gt))
            did(V.scalar_tensor_tensor(padsel[:], toolow[:], anyrow[:, 0:1], legrow[:], ALU.mult, ALU.add))
            did(V.tensor_copy(eidi[:], eid[:]))
            did(V.tensor_scalar(eids[:], eidi[:], RW - 1, None, ALU.bitwise_and))
            did(V.tensor_copy(eidf[:], eids[:]))
            V.tensor_scalar(tcol[:, RING, :], eidf[:], float(WE), None, ALU.mult).then_inc(tcol_ready, 1)
            V.tensor_copy(tab_pad[:], padsel[0:1, :]).then_inc(tab_ready, 1)
            V.tensor_copy(tab_end[:], cum[0:1, :]).then_inc(tab_ready, 1)
            dve.wait_ge(tab_rows, 1)
            V.tensor_copy(tab[:], psum[0:1, 0:4, :].rearrange("p b n -> p (b n)")[:, 0:NQ * TC * P]).then_inc(tab_ready, 1)
            dve.wait_ge(tab_ready, 3)

            def step(t, q):
                a = t + 3
                if real(a):
                    qa = (q + 3) % 4
                    dve.wait_ge(xhi_ready, a + 1)
                    V.tensor_tensor(xlo[qa][:], bX[(q + 3) % 2], xhi[qa][:].bitcast(fp32), ALU.subtract).then_inc(xlo_ready, 1)
                a = t + 1
                if real(a):
                    qa = (q + 1) % 8
                    dve.wait_ge(silu_ready, a + 1)
                    reached(dve, hT_ready, a - 1)
                    V.tensor_tensor(ht[qa % 2][:], sgt[qa % 2][:], bG[qa % 2][:, F:2 * F], ALU.mult).then_inc(h_ready, 1)
                a = t
                if real(a):
                    qa = q
                    dve.wait_ge(hT_ready, a + 1)
                    reached(dve, o_ready, a)
                    V.tensor_copy(hhi[qa % 2][:], bH[qa % 2]).then_inc(hhi_ready, 1)
                    dve.wait_ge(hhi_ready, a + 1)
                    V.tensor_tensor(hlo[qa % 2][:], bH[qa % 2], hhi[qa % 2][:].bitcast(fp32), ALU.subtract).then_inc(hlo_ready, 1)

            tiles(dve, step, lead=3, lag=1)

            def stage(j, q):
                dveI.begin(j)
                def of(all_):
                    return all_[:].rearrange("p b (u k) -> p (b u) k", u=U)[:, bass.ds(j, 1), :].rearrange("p a k -> p (a k)")
                V.tensor_copy(wk[q][:], of(wkall)).then_inc(wk_ready, 1)
                s = dveI.did(V.tensor_copy(pk[q][:], of(placeall)))
                dveI.wait(dve, s)
                for k in range(K):
                    s = dveI.did(V.scalar_tensor_tensor(moves[:, k, :], place0[:], pk[q][:, k:k + 1], move[:], ALU.is_le,
                                                        ALU.mult, accum_out=moved[q][:, k:k + 1]))
                dveI.wait(dve, s)
                V.scalar_tensor_tensor(idxs[q][:], moved[q][:], -1.0, pk[q][:], ALU.add, ALU.add).then_inc(idxs_ready, 1)
                dveI.end()

            def combine(j, q, i):
                dveC.begin(j)
                dve.wait_ge(wk_ready, j + 1)
                dve.wait_ge(gathered[q], 16 * K * (i + 1))
                before = ysh[:, bass.ds(j, 1), :].rearrange("p a d -> p (a d)")
                for k in range(K):
                    s = dveC.did(V.scalar_tensor_tensor(acc[:, k % 2, :], got[q][:, k, :], wk[q][:, k:k + 1], before,
                                                        ALU.mult, ALU.add))
                    dveC.wait(dve, s)
                    before = acc[:, k % 2, :]
                reached(dve, res_stored[q], 16 * i)
                V.scalar_tensor_tensor(res[q][:], before, gate_t[:, 1:2], x2[:, bass.ds(j, 1), :].rearrange("p a d -> p (a d)"),
                                       ALU.mult, ALU.add).then_inc(res_ready, 1)
                dveC.end()
                if not (isinstance(j, int) and j + 2 >= NT):
                    stage(j + 2, q)

            stage(0, 0)
            stage(1, 1)
            for j in range(2):
                combine(j, j, 0)
            with dve.Fori(1, NT // 2 - 1) as i:
                for q in range(2):
                    combine(2 * i + q, q, i)
            for j in range(NT - 2, NT):
                combine(j, j % 2, NT // 2 - 1)

        block = ex.enter_context(nc.Block())

        def passes(engine, one_pass):
            def batch(p, q, i, lag):
                if isinstance(p, int) and not 0 <= p - lag < B:
                    return None
                return (p - lag, (q - lag) % 2, i - (lag + 1 - q) // 2 if lag else i)

            def run(p, q, i):
                one_pass(batch(p, q, i, 0), batch(p, q, i, 1), batch(p, q, i, 2))

            for p in range(4):
                run(p, p % 2, p // 2)
            with engine.Fori(2, NB) as i:
                for q in range(2):
                    run(2 * i + q, q, i)
            for p in range(B, B + 2):
                run(p, p % 2, p // 2)

        @block.sync
        def _(sp):
            for dst, src in ((wg[:], w_gates), (lnw[:], ln_weight.partition_broadcast(P)),
                             (gbias[:], b_gates.partition_broadcast(P)),
                             (rbias[:], b_router.partition_broadcast(P)),
                             (gate_in[:, 0:1], g_xattn.partition_broadcast(P)),
                             (gate_in[:, 1:2], g_ffn.partition_broadcast(P)),
                             (wr[:], w_router.rearrange("(k p) e -> p k e", p=P)),
                             (wsg[:], ws_gate.rearrange("(k p) f -> p k f", p=P)),
                             (wsu[:], ws_up.rearrange("(k p) f -> p k f", p=P)),
                             (wsd[:], ws_down)):
                sp.dma_start(dst, src).then_inc(s_small, 16)
            xv = x.rearrange("b (u p) d -> b p u d", p=P)
            cv = ctx.rearrange("b (u p) d -> b p u d", p=P)

            def load(gates, heads, route):
                if gates is None:
                    return
                b, par, n = gates
                reached(sp, x2_ready, b - 1)
                sp.dma_start(xin[par][:], xv[bass.ds(b, 1)].rearrange("a p u d -> p (a u) d")).then_inc(x_loaded[par], 16)
                reached(sp, ctx_transposed, b - 1)
                reached(sp, vext_ready, b - 1)
                sp.dma_start(cin[par][:], cv[bass.ds(b, 1)].rearrange("a p u d -> p (a u) d")).then_inc(c_loaded[par], 16)

            sp.wait_ge(s_const, 14)
            for e0 in range(0, E, 16):
                sp.dma_start(xs.rearrange("(e r) d -> r e d", e=E)[REG - P:REG, e0:e0 + 16, :],
                             zrow[:].unsqueeze(1).to_broadcast([P, 16, D])).then_inc(ends_zeroed, 16)
            passes(sp, load)
            phase2_sp(sp)

        @block.gpsimd
        def _(pool):
            for m, v in ((ident, 0.0), (identb, 0.0), (tri_inc, 1.0), (tri_exc, 1.0), (ones, 1.0),
                         (onesb, 1.0), (mask, -1e30), (head_row, 0.0), (zeros4, 0.0), (zrow, 0.0),
                         (earlier, 1.0), (later, 1.0), (vext[0], 1.0), (vext[1], 1.0)):
                nc.gpsimd.memset(m[:], v).then_inc(s_const, 1)
            pool.wait_ge(s_const, 14)
            sel = nc.gpsimd.affine_select
            for m in (ident, identb):
                sel(out=m[:], in_=m[:], compare_op=ALU.not_equal, fill=1.0, base=0,
                    pattern=[[-1, P]], channel_multiplier=1).then_inc(s_const, 1)
            sel(out=tri_inc[:], in_=tri_inc[:], compare_op=ALU.is_ge, fill=0.0, base=0,
                pattern=[[1, P]], channel_multiplier=-1).then_inc(s_const, 1)
            sel(out=tri_exc[:], in_=tri_exc[:], compare_op=ALU.is_gt, fill=0.0, base=0,
                pattern=[[1, P]], channel_multiplier=-1).then_inc(s_const, 1)
            sel(out=mask[:], in_=mask[:], compare_op=ALU.is_gt, fill=0.0, base=0,
                pattern=[[-1, P]], channel_multiplier=1).then_inc(s_const, 1)
            sel(out=head_row[:], in_=head_row[:], compare_op=ALU.not_equal, fill=1.0, base=0,
                pattern=[[-1, NH], [0, P]], channel_multiplier=1).then_inc(s_const, 1)
            sel(out=earlier[:], in_=earlier[:], compare_op=ALU.is_gt, fill=0.0, base=0,
                pattern=[[1, NG], [-1, NG]], channel_multiplier=0).then_inc(s_const, 1)
            sel(out=later[:], in_=later[:], compare_op=ALU.is_gt, fill=0.0, base=0,
                pattern=[[-1, NG], [1, NG]], channel_multiplier=0).then_inc(s_const, 1)
            for m in (place, place0):
                nc.gpsimd.iota(m[:], pattern=[[REG, E]], base=1, channel_multiplier=0,
                               allow_small_or_imprecise_dtypes=True).then_inc(s_const, 1)
            nc.gpsimd.iota(tno[:], pattern=[[P, TC]], base=0, channel_multiplier=1,
                           allow_small_or_imprecise_dtypes=True).then_inc(s_const, 1)

            pool.wait_ge(ends_zeroed, 64)
            nc.gpsimd.sem_inc(pool_mark, 1)

            def scatter(gates, heads, route):
                if route is None:
                    return
                b, par, n = route
                pool.wait_ge(idx_ready, b + 1)
                nc.gpsimd.sem_inc(pool_mark, 1)
                pool.wait_ge(row_ready, U * (b + 1))
                nc.gpsimd.sem_inc(pool_mark, 1)
                for u in range(U):
                    for k in range(K):
                        nc.gpsimd.indirect_dma_start(
                            out=xs, out_offset=bass.IndirectOffsetOnAxis(ap=idx[par][:, u * K + k:u * K + k + 1], axis=0),
                            in_=rows[par][:, u, :], in_offset=None).then_inc(scattered[par], 16)

            passes(pool, scatter)
            phase2_pool(pool)

        CONST = 14 + 8 + 3

        @block.tensor
        def _(pe):
            pe.wait_ge(s_const, CONST)
            pe.wait_ge(s_ready0, 1)
            pe.wait_ge(s_small, 160)
            mm, tr = nc.tensor.matmul, nc.tensor.transpose

            def ctx_t(g):
                b, par, n = g
                pe.wait_ge(c_loaded[par], 16 * (n + 1))
                reached(pe, nmd_ready, b)
                for k in range(KC):
                    for u in range(U):
                        last = tr(bT[:, k * S + u * P:k * S + (u + 1) * P], cin[par][:, u, k * P:(k + 1) * P], ident[:])
                last.then_inc(ctx_transposed, 1)

            def xn_t(g):
                b, par, n = g
                pe.wait_ge(ctxT_ready, b + 1)
                pe.wait_ge(xn_ready, U * (b + 1))
                for k in range(KC):
                    for u in range(U):
                        last = tr(bT[:, k * S + u * P:k * S + (u + 1) * P], xn[:, u, k * P:(k + 1) * P], ident[:])
                last.then_inc(xn_transposed, 1)

            def gate_mm(g):
                b, par, n = g
                pe.wait_ge(xnT_ready, b + 1)
                for u in range(U):
                    dst = bT[:, u * 2 * NH:(u + 1) * 2 * NH]
                    for k in range(KC):
                        mm(dst, xnT[par][:, k, u * P:(u + 1) * P], wg[:, k, :], start=k == 0, stop=False)
                    for k in range(KC):
                        last = mm(dst, ctxT[par][:, k, u * P:(u + 1) * P], wctx[:, k, :], start=False, stop=k == KC - 1)
                last.then_inc(gates_ready, 1)

            def cum_mm(g):
                b, par, n = g
                pe.wait_ge(logf_ready, b + 1)
                mm(bT[:, 16:20], tri_inc[:], lf[:, 0, :], start=True, stop=True)
                mm(bT[:, 20:24], tri_inc[:], lf[:, 1, :], start=True, stop=False)
                mm(bT[:, 20:24], ones[:], lf[:, 0, :], start=False, stop=True).then_inc(cumf_ready, 1)

            def ng_t(g):
                b, par, n = g
                pe.wait_ge(ng_ready, b + 1)
                for u in range(U):
                    last = tr(bT[0:NH, 32 + u * P:32 + (u + 1) * P], ng[:, u, :], ident[:])
                last.then_inc(ngT_ready, 1)

            def negm_t(g):
                b, par, n = g
                pe.wait_ge(negm_ready, b + 1)
                for u in range(U):
                    last = mm(bT[:, 24 + u * NH:24 + (u + 1) * NH], negm[par][:, u * P:(u + 1) * P], ident[0:NH, 0:NH],
                              start=True, stop=True)
                last.then_inc(negm_cols_ready, 1)

            def qk(hd, h):
                b, par, n = hd
                r = slice((h % 2) * DH, (h % 2) * DH + DH)
                reached(pe, cmat_ready, NH * b + h - 1)
                mm(bS[h % 2][:, 0:S], ctxT[par][r, h // 2, 0:P], xnT[par][r, h // 2, :], start=True, stop=True)
                mm(bS[h % 2][:, S:S + P], ctxT[par][r, h // 2, P:S], xnT[par][r, h // 2, P:S],
                   start=True, stop=True).then_inc(scores_ready, 1)
                reached(pe, decay_ready, NH * b + h)
                if h == 0:
                    pe.wait_ge(negm_ready, b + 1)
                mm(bM[:, 0:P], head_row[:, h, :], negm[par][:, 0:P], start=True, stop=False)
                mm(bM[:, 0:P], identb[:], mask[:], start=False, stop=True)
                mm(bM[:, P:S], head_row[:, h, :], negm[par][:, P:S], start=True, stop=True)
                mm(bM[:, S:S + P], head_row[:, h, :], negm[par][:, P:S], start=True, stop=False)
                mm(bM[:, S:S + P], identb[:], mask[:], start=False, stop=True).then_inc(decay_arg_ready, 1)

            def av(hd, h):
                b, par, n = hd
                if h == 0:
                    pe.wait_ge(vext_ready, b + 1)
                    reached(pe, hst_done, b)
                pe.wait_ge(cmat_ready, NH * b + h + 1)
                c, o = cmat[h % 2], slice(h * (DH + 1), (h + 1) * (DH + 1))
                mm(bAV[0][:, o], c[:, 0:P], vext[par][:, 0, h, :], start=True, stop=True)
                mm(bAV[1][:, o], c[:, P:S], vext[par][:, 0, h, :], start=True, stop=False)
                mm(bAV[1][:, o], c[:, S:S + P], vext[par][:, 1, h, :], start=False, stop=True).then_inc(av_done, 1)

            def x2_t(rt):
                b, par, n = rt
                pe.wait_ge(row_ready, U * (b + 1))
                reached(pe, ysh_done, b)
                for k in range(KC):
                    for u in range(U):
                        last = tr(bB0[:, k * S + u * P:k * S + (u + 1) * P], rows[par][:, u, k * P:(k + 1) * P], ident[:])
                last.then_inc(x2_transposed, 1)

            def router(rt):
                b, par, n = rt
                pe.wait_ge(x2T_ready, b + 1)
                reached(pe, place_done, b)
                for u in range(U):
                    for k in range(KC):
                        last = mm(bB1[:, u * E:(u + 1) * E], x2T[:, k, u * P:(u + 1) * P], wr[:, k, :],
                                  start=k == 0, stop=k == KC - 1)
                last.then_inc(logits_ready, 1)

            def shared_up(rt):
                for o, w in ((0, wsg), (S, wsu)):
                    for k in range(KC):
                        last = mm(bB0[:, o:o + S], w[:, k, :], x2T[:, k, :], start=k == 0, stop=k == KC - 1)
                last.then_inc(gu_ready, 1)

            def shared_down(rt):
                b, par, n = rt
                pe.wait_ge(hs_ready, b + 1)
                for u in range(U):
                    last = mm(bB0[:, u * D:(u + 1) * D], hs[:, u * P:(u + 1) * P], wsd[:], start=True, stop=True)
                last.then_inc(y_ready, 1)

            def ranks(rt):
                b, par, n = rt
                pe.wait_ge(chosen_ready, b + 1)
                mm(bB1[:, 128:128 + E], tri_exc[:], chosen[:, 0, :], start=True, stop=True)
                mm(bB1[:, 128 + E:128 + 2 * E], tri_exc[:], chosen[:, 1, :], start=True, stop=False)
                mm(bB1[:, 128 + E:128 + 2 * E], onesb[:], chosen[:, 0, :], start=False, stop=True)
                mm(bB1[:, 256:256 + E], onesb[:], chosen[:, 0, :], start=True, stop=False)
                mm(bB1[:, 256:256 + E], onesb[:], chosen[:, 1, :], start=False, stop=True).then_inc(ranks_ready, 1)

            def one(g, hd, rt):
                if g: ctx_t(g)
                if hd: qk(hd, 0)
                if rt: x2_t(rt)
                if g: xn_t(g)
                if hd: qk(hd, 1); av(hd, 0)
                if rt: router(rt); shared_up(rt)
                if g: gate_mm(g)
                if hd: qk(hd, 2); av(hd, 1)
                if g: cum_mm(g)
                if hd: qk(hd, 3); av(hd, 2)
                if rt: ranks(rt)
                if g: ng_t(g)
                if rt: shared_down(rt)
                if hd: av(hd, 3)
                if g: negm_t(g)

            passes(pe, one)
            phase2_pe(pe)

        @block.scalar
        def _(act):
            A = nc.scalar.activation
            act.wait_ge(s_small, 160)
            A(gate_t[:], gate_in[:], ACT.Tanh).then_inc(s_tanh, 1)
            act.wait_ge(s_const, CONST)
            act.wait_ge(s_tanh, 1)
            act.add_instruction(mybir.InstLoadActFuncSet(name=nc.get_next_instruction_name(), act_func_set_id=EXP_AND_LN,
                                                         ins=[], outs=[]))

            def ctx_copy(g):
                b, par, n = g
                reached(act, av_done, NH * (b - 1))
                act.wait_ge(ctx_transposed, b + 1)
                A(ctxT[par][:].rearrange("p k s -> p (k s)"), bT[:, 0:KC * S], ACT.Copy).then_inc(ctxT_ready, 1)
                act.wait_ge(c_loaded[par], 16 * (n + 1))
                A(vext[par][:, :, :, 0:DH], cin[par][:].rearrange("p u (h d) -> p u h d", h=NH),
                  ACT.Copy).then_inc(vext_ready, 1)

            def guess(steps, ready, var, ln, r, out_sem, b):
                act.wait_ge(ready, b + 1)
                s = steps.did(A(ln[:], var[:], ACT.Ln))
                steps.wait(act, s)
                A(r[:], ln[:], ACT.Exp, scale=-0.5).then_inc(out_sem, 1)

            def xn_copy(g):
                b, par, n = g
                act.wait_ge(xn_transposed, b + 1)
                A(xnT[par][:].rearrange("p k s -> p (k s)"), bT[:, 0:KC * S], ACT.Copy).then_inc(xnT_ready, 1)

            def softplus(g):
                b, par, n = g
                act.wait_ge(absf_ready, b + 1)
                s = actG.did(A(expf[:], absf[:], ACT.Exp, scale=-1.0))
                actG.wait(act, s)
                A(sp[:], expf[:], ACT.Ln, bias=1.0).then_inc(softplus_ready, 1)

            def exp_negm(g):
                b, par, n = g
                act.wait_ge(nmd_ready, b + 1)
                A(enm[par][:], nmd[:], ACT.Exp).then_inc(enm_ready, 1)

            def decay_exp(hd, h):
                b, par, n = hd
                if h == 0:
                    act.wait_ge(gcol_ready, b + 1)
                reached(act, cmat_ready, NH * b + h - 1)
                act.wait_ge(decay_arg_ready, NH * b + h + 1)
                A(decay[h % 2][:, 0:S], bM[:, 0:S], ACT.Exp, bias=gcol[par][:, 0, h:h + 1])
                A(decay[h % 2][:, S:S + P], bM[:, S:S + P], ACT.Exp,
                  bias=gcol[par][:, 1, h:h + 1]).then_inc(decay_ready, 1)

            def x2_keep(rt):
                b, par, n = rt
                act.wait_ge(x2_ready, b + 1)
                A(x2[:, bass.ds(U * b, U), :], x2now[par][:], ACT.Copy).then_inc(x2_kept, 1)

            def x2_copy(rt):
                b, par, n = rt
                act.wait_ge(x2_transposed, b + 1)
                reached(act, gu_ready, b)
                A(x2T[:].rearrange("p k s -> p (k s)"), bB0[:, 0:KC * S], ACT.Copy).then_inc(x2T_ready, 1)

            def router_exp(rt):
                b, par, n = rt
                act.wait_ge(logits_ready, b + 1)
                A(es[:].rearrange("p u e -> p (u e)"), bB1[:, 0:U * E], ACT.Exp, scale=-1.0).then_inc(es_ready, 1)
                act.wait_ge(gu_ready, b + 1)
                A(eg[:], bB0[:, 0:S], ACT.Exp, scale=-1.0).then_inc(eg_ready, 1)

            def shared_copy(rt):
                b, par, n = rt
                act.wait_ge(y_ready, b + 1)
                A(ysh[:, bass.ds(U * b, U), :].rearrange("p u d -> p (u d)"), bB0[:, 0:U * D],
                  ACT.Copy).then_inc(ysh_done, 1)

            def one(g, hd, rt):
                if g: actG.begin(g[0])
                if hd: actH.begin(hd[0])
                if rt: actL.begin(rt[0])
                if g: ctx_copy(g); guess(actG, var1_ready, ve1, ln1, r1, guess1_ready, g[0])
                if hd: decay_exp(hd, 0)
                if rt: guess(actL, var3_ready, ve3, ln3, r3, guess3_ready, rt[0]); x2_copy(rt)
                if g: xn_copy(g)
                if hd: decay_exp(hd, 1)
                if rt: router_exp(rt); x2_keep(rt)
                if hd: decay_exp(hd, 2)
                if g: softplus(g)
                if hd: decay_exp(hd, 3)
                if rt: shared_copy(rt)
                if g: exp_negm(g)
                if hd: guess(actH, var2_ready, ve2, ln2, r2, guess2_ready, hd[0])
                for steps, x_ in ((actG, g), (actH, hd), (actL, rt)):
                    if x_: steps.end()

            passes(act, one)
            phase2_act(act)

        @block.vector
        def _(dve):
            V = nc.vector
            dve.wait_ge(s_small, 160)
            dve.wait_ge(s_tanh, 1)
            V.tensor_tensor(wctx[:], wg[:, KC:2 * KC, :], wg[:, 2 * KC:3 * KC, :], ALU.add).then_inc(s_ready0, 1)
            V.tensor_scalar(wt[:], lnw[:], 1.0, gate_t[:, 0:1], ALU.add, ALU.mult).then_inc(s_constv, 1)
            dve.wait_ge(s_constv, 1)
            dve.wait_ge(s_const, CONST)

            def newton(st, var, r, t, rstd, guess_sem, b):
                dve.wait_ge(guess_sem, b + 1)
                s = st.did(V.tensor_tensor(t[:], var[:], r[:], ALU.mult))
                st.wait(dve, s)
                s = st.did(V.scalar_tensor_tensor(t[:], t[:], -0.5, r[:], ALU.mult, ALU.mult))
                st.wait(dve, s)
                return st.did(V.scalar_tensor_tensor(rstd[:], t[:], 1.5, r[:], ALU.add, ALU.mult))

            def stats(st, stt, mv, var, src, var_sem):
                V.sem_inc(dve_mark, 1)
                for u in range(U):
                    s = st.did(V.bn_stats(stt[:, u, :], src(u)))
                st.wait(dve, s)
                V.sem_inc(dve_mark, 1)
                for u in range(U):
                    s = st.did(V.bn_aggr(mv[:, u, :], stt[:, u, :]))
                st.wait(dve, s)
                V.tensor_scalar(var[:], mv[:, :, 1], EPS_LN, None, ALU.add).then_inc(var_sem, 1)

            def gates_stats(g):
                b, par, n = g
                dve.wait_ge(x_loaded[par], 16 * (n + 1))
                stats(dveG, st1, mv1, ve1, lambda u: xin[par][:, u, :], var1_ready)

            def gates_norm(g):
                b, par, n = g
                s = newton(dveG, ve1, r1, t1, rstd1, guess1_ready, b)
                reached(dve, xn_transposed, b)
                dveG.wait(dve, s)
                for u in range(U):
                    V.tensor_scalar(xn[:, u, :], xin[par][:, u, :], mv1[:, u, 0:1], rstd1[:, u:u + 1],
                                    ALU.subtract, ALU.mult).then_inc(xn_ready, 1)

            def gates_abs(g):
                b, par, n = g
                dve.wait_ge(gates_ready, b + 1)
                s = dveG.did(V.tensor_tensor(gate[:], bT[:, 0:U * 2 * NH].rearrange("p (u h) -> p u h", u=U),
                                             gbias[:].unsqueeze(1).to_broadcast([P, U, 2 * NH]), ALU.add))
                dveG.wait(dve, s)
                V.scalar_tensor_tensor(absf[:], gate[:, :, NH:], -1.0, gate[:, :, NH:], ALU.mult, ALU.max).then_inc(absf_ready, 1)

            def gates_logf(g):
                b, par, n = g
                dve.wait_ge(softplus_ready, b + 1)
                V.scalar_tensor_tensor(lf[:], gate[:, :, NH:], 0.0, sp[:], ALU.min, ALU.subtract).then_inc(logf_ready, 1)

            def gates_ng(g):
                b, par, n = g
                dve.wait_ge(cumf_ready, b + 1)
                cum_v = bT[:, 16:24].rearrange("p (u h) -> p u h", u=U)
                s = dveG.did(V.tensor_copy(cfs[:], cum_v))
                V.tensor_tensor(ng[:], cum_v, gate[:, :, 0:NH], ALU.subtract).then_inc(ng_ready, 1)
                dve.wait_ge(ng_ready, b + 1)
                reached(dve, av_done, NH * (b - 1))
                V.tensor_scalar(gcol[par][:], ng[:], -1.0, None, ALU.mult).then_inc(gcol_ready, 1)
                return s

            def gates_scan(g, s):
                b, par, n = g
                dve.wait_ge(ngT_ready, b + 1)
                V.tensor_tensor_scan(negm[par][:], bT[0:NH, 32:32 + S], zeros4[:], BIG, ALU.min, ALU.add).then_inc(negm_ready, 1)
                dve.wait_ge(negm_cols_ready, b + 1)
                dveG.wait(dve, s)
                V.tensor_tensor(nmd[:], bT[:, 24:32].rearrange("p (u h) -> p u h", u=U), cfs[:],
                                ALU.subtract).then_inc(nmd_ready, 1)

            def head(hd, h):
                b, par, n = hd
                dve.wait_ge(scores_ready, NH * b + h + 1)
                reached(dve, av_done, NH * b + h - 1)
                dve.wait_ge(decay_ready, NH * b + h + 1)
                V.scalar_tensor_tensor(cmat[h % 2][:], bS[h % 2][:, 0:S + P], float(DH) ** -0.5, decay[h % 2][:],
                                       ALU.mult, ALU.mult).then_inc(cmat_ready, 1)

            def heads_out(hd):
                b, par, n = hd
                dve.wait_ge(enm_ready, b + 1)
                dve.wait_ge(av_done, NH * (b + 1))
                avv = [bAV[u][:, 0:NH * (DH + 1)].rearrange("p (h d) -> p h d", h=NH) for u in range(U)]
                for u in range(U):
                    s = dveH.did(V.scalar_tensor_tensor(floor_[:, u, :], avv[u][:, :, DH], -1.0, enm[par][:, u, :],
                                                        ALU.mult, ALU.max))
                dveH.wait(dve, s)
                for u in range(U):
                    s = dveH.did(V.tensor_tensor(den[:, u, :], avv[u][:, :, DH], floor_[:, u, :], ALU.max))
                dveH.wait(dve, s)
                s = dveH.did(V.tensor_scalar(deneps[:], den[:], 1e-6, None, ALU.add))
                dveH.wait(dve, s)
                s = dveH.did(V.reciprocal(rden[:], deneps[:]))
                dveH.wait(dve, s)
                for u in range(U):
                    read = V.tensor_tensor(hst[:, u * NH:(u + 1) * NH, :], avv[u][:, :, 0:DH],
                                           rden[:, u, :].unsqueeze(2).to_broadcast([P, NH, DH]), ALU.mult)
                    if u == 0:
                        s = dveH.did(read)
                    else:
                        read.then_inc(hst_done, 1)
                dveH.wait(dve, s)
                dve.wait_ge(hst_done, b + 1)
                V.sem_inc(dve_mark, 1)
                for j in range(U * NH):
                    s = dveH.did(V.bn_stats(st2[:, j, :], hst[:, j, :]))
                dveH.wait(dve, s)
                a = dveH.did(V.tensor_tensor(dm2[:], st2[:, :, 1], st2[:, :, 4], ALU.subtract))
                c = dveH.did(V.tensor_tensor(m2[:], st2[:, :, 2], st2[:, :, 5], ALU.add))
                d = dveH.did(V.tensor_tensor(sm2[:], st2[:, :, 1], st2[:, :, 4], ALU.add))
                dveH.wait(dve, a)
                s = dveH.did(V.scalar_tensor_tensor(q2[:], dm2[:], 0.25, dm2[:], ALU.mult, ALU.mult))
                dveH.wait(dve, s)
                s = dveH.did(V.scalar_tensor_tensor(v2[:], m2[:], 1.0 / DH, q2[:], ALU.mult, ALU.add))
                dveH.wait(dve, s)
                V.tensor_scalar(ve2[:], v2[:], EPS_LN, None, ALU.add).then_inc(var2_ready, 1)
                s = dveH.did(V.tensor_scalar(mean2[:], sm2[:], 0.5, None, ALU.mult))
                dveH.wait(dve, s)
                dveH.did(V.tensor_tensor(hc[:], hst[:], mean2[:].unsqueeze(2).to_broadcast([P, U * NH, DH]),
                                         ALU.subtract))

            def heads_norm(hd):
                b, par, n = hd
                s = newton(dveH, ve2, r2, t2, rstd2, guess2_ready, b)
                dveH.wait(dve, s)
                s = dveH.did(V.tensor_tensor(hn[:], hc[:], rstd2[:].unsqueeze(2).to_broadcast([P, U * NH, DH]), ALU.mult))
                dveH.wait(dve, s)
                s = dveH.did(V.tensor_tensor(hw[:].rearrange("p (u h) d -> p u (h d)", u=U),
                                             hn[:].rearrange("p (u h) d -> p u (h d)", u=U),
                                             wt[:].unsqueeze(1).to_broadcast([P, U, D]), ALU.mult))
                dveH.wait(dve, s)
                reached(dve, x2_kept, b - 1)
                V.tensor_tensor(x2now[par][:], hw[:].rearrange("p (u h) d -> p u (h d)", u=U),
                                xin[par][:], ALU.add).then_inc(x2_ready, 1)

            def route_stats(rt):
                b, par, n = rt
                dve.wait_ge(x2_ready, b + 1)
                stats(dveL, st3, mv3, ve3, lambda u: x2now[par][:, u, :], var3_ready)

            def route_norm(rt):
                b, par, n = rt
                s = newton(dveL, ve3, r3, t3, rstd3, guess3_ready, b)
                reached(dve, scattered[par], U * K * 16 * n)
                dveL.wait(dve, s)
                for u in range(U):
                    V.tensor_scalar(rows[par][:, u, :], x2now[par][:, u, :],
                                    mv3[:, u, 0:1], rstd3[:, u:u + 1], ALU.subtract, ALU.mult).then_inc(row_ready, 1)

            def route_score(rt):
                b, par, n = rt
                dve.wait_ge(es_ready, b + 1)
                s = dveL.did(V.tensor_scalar(es1[:], es[:], 1.0, None, ALU.add))
                dveL.wait(dve, s)
                s = dveL.did(V.reciprocal(score[:], es1[:]))
                dveL.wait(dve, s)
                s = dveL.did(V.tensor_tensor(biased[:], score[:], rbias[:].unsqueeze(1).to_broadcast([P, U, E]), ALU.add))
                dveL.wait(dve, s)
                bg = biased[:].rearrange("p u (g i) -> p (u g) i", g=NG)
                V.sem_inc(dve_mark, 1)
                for j in range(U * NG):
                    s = dveL.did(V.max(top_in_group[:, j, :], bg[:, j, :]))
                dveL.wait(dve, s)
                gs = gscore[:].rearrange("p u g -> p (u g)")
                s = dveL.did(V.tensor_tensor(gs, top_in_group[:, :, 0], top_in_group[:, :, 1], ALU.add))
                dveL.wait(dve, s)

            def route_groups(rt):
                a = U * NG
                other = gscore[:].unsqueeze(2).to_broadcast([P, U, NG, NG])
                own = gscore[:].unsqueeze(3).to_broadcast([P, U, NG, NG])
                s = dveL.did(V.tensor_tensor(gge[:], other, own, ALU.is_ge))
                t = dveL.did(V.tensor_tensor(ggt[:], other, own, ALU.is_gt))
                dveL.wait(dve, s)
                s = dveL.did(V.tensor_tensor(gge[:], gge[:], earlier[:].unsqueeze(1).to_broadcast([P, U, NG, NG]), ALU.mult))
                dveL.wait(dve, t)
                t = dveL.did(V.tensor_tensor(ggt[:], ggt[:], later[:].unsqueeze(1).to_broadcast([P, U, NG, NG]), ALU.mult))
                dveL.wait(dve, t)
                s = dveL.did(V.tensor_tensor(grank3[:], gge[:], ggt[:], ALU.add))
                dveL.wait(dve, s)
                s = dveL.did(V.tensor_reduce(grank[:].rearrange("p u g -> p (u g)"),
                                             grank3[:].rearrange("p u g h -> p (u g) h"), AX.X, ALU.add))
                dveL.wait(dve, s)
                s = dveL.did(V.tensor_scalar(gmask[:], grank[:], float(TOPG) - 0.5, None, ALU.is_lt))
                dveL.wait(dve, s)
                s = dveL.did(V.tensor_tensor(masked[:].rearrange("p u (g i) -> p (u g) i", g=NG),
                                             biased[:].rearrange("p u (g i) -> p (u g) i", g=NG),
                                             gmask[:].rearrange("p u g -> p (u g)").unsqueeze(2).to_broadcast([P, U * NG, GS]),
                                             ALU.mult))
                dveL.wait(dve, s)
                V.sem_inc(dve_mark, 1)
                for u in range(U):
                    s = dveL.did(V.max(top[:, u, :], masked[:, u, :]))
                dveL.wait(dve, s)
                V.sem_inc(dve_mark, 1)
                for u in range(U):
                    s = dveL.did(V.match_replace(repl[:, u, :], top[:, u, :], masked[:, u, :], -BIG))
                dveL.wait(dve, s)
                V.tensor_tensor(chosen[:], repl[:], masked[:], ALU.not_equal).then_inc(chosen_ready, 1)

            def route_weights(rt):
                b, par, n = rt
                dve.wait_ge(chosen_ready, b + 1)
                s = dveL.did(V.tensor_tensor(wsel[:], score[:], chosen[:], ALU.mult))
                dveL.wait(dve, s)
                s = dveL.did(V.tensor_reduce(wsum[:], wsel[:], AX.X, ALU.add))
                dveL.wait(dve, s)
                s = dveL.did(V.tensor_scalar(wsume[:], wsum[:], 1e-20, None, ALU.add))
                dveL.wait(dve, s)
                s = dveL.did(V.reciprocal(wrec[:], wsume[:]))
                dveL.wait(dve, s)
                for u in range(U):
                    s = dveL.did(V.tensor_scalar(wn[:, u, :], wsel[:, u, :], wrec[:, u:u + 1], 2.5, ALU.mult, ALU.mult))
                return s

            def route_place(rt, weights):
                b, par, n = rt
                dve.wait_ge(ranks_ready, b + 1)
                rk = bB1[:, 128:128 + U * E].rearrange("p (u e) -> p u e", u=U)
                reached(dve, place_done, b)
                s = dveL.did(V.tensor_tensor(pos[:], rk, place[:].unsqueeze(1).to_broadcast([P, U, E]), ALU.add))
                dveL.wait(dve, s)
                V.tensor_tensor(place[:], place[:], bB1[:, 256:256 + E], ALU.add).then_inc(place_done, 1)
                s = dveL.did(V.tensor_tensor(posm[:], pos[:], chosen[:], ALU.mult))
                dveL.wait(dve, s)
                V.sem_inc(dve_mark, 1)
                for u in range(U):
                    s = dveL.did(V.max(place8[:, u, :], posm[:, u, :]))
                dveL.wait(dve, s)
                p8 = place8[:].rearrange("p u k -> p (u k)")
                V.tensor_scalar(idx[par][:], p8, -1.0, None, ALU.add).then_inc(idx_ready, 1)
                dveL.did(V.tensor_copy(placeall[:, bass.ds(b, 1), :].rearrange("p a k -> p (a k)"), p8))
                dveL.wait(dve, weights)
                for u in range(U):
                    for k in range(K):
                        dveL.did(V.scalar_tensor_tensor(
                            picked[:, u * K + k, :], posm[:, u, :], place8[:, u, k:k + 1], wn[:, u, :], ALU.is_equal, ALU.mult,
                            accum_out=wkall[:, bass.ds(b, 1), u * K + k:u * K + k + 1].rearrange("p a k -> p (a k)")))

            def shared_silu(rt):
                b, par, n = rt
                dve.wait_ge(eg_ready, b + 1)
                s = dveL.did(V.tensor_scalar(eg1[:], eg[:], 1.0, None, ALU.add))
                dveL.wait(dve, s)
                s = dveL.did(V.reciprocal(sg[:], eg1[:]))
                dveL.wait(dve, s)
                s = dveL.did(V.tensor_tensor(hg[:], bB0[:, 0:S], sg[:], ALU.mult))
                reached(dve, y_ready, b)
                dveL.wait(dve, s)
                V.tensor_tensor(hs[:], bB0[:, S:2 * S], hg[:], ALU.mult).then_inc(hs_ready, 1)

            def one(g, hd, rt):
                if g: dveG.begin(g[0])
                if hd: dveH.begin(hd[0])
                if rt: dveL.begin(rt[0])
                if rt: route_stats(rt)
                if g: gates_stats(g)
                if hd: head(hd, 0)
                if rt: route_norm(rt)
                if g: gates_norm(g)
                if hd: head(hd, 1)
                if rt: route_score(rt)
                if g: gates_abs(g)
                if hd: head(hd, 2)
                if g: gates_logf(g)
                if rt: route_groups(rt)
                if g: s = gates_ng(g)
                if hd: head(hd, 3)
                if rt: shared_silu(rt); route_place(rt, route_weights(rt))
                if g: gates_scan(g, s)
                if hd: heads_out(hd); heads_norm(hd)
                for steps, x_ in ((dveG, g), (dveH, hd), (dveL, rt)):
                    if x_: steps.end()

            passes(dve, one)
            phase2_dve(dve)


def kernel(x, ctx_1024, g_xattn, g_ffn, L0_xattn_w_igate, L0_xattn_b_igate, L0_xattn_w_fgate,
           L0_xattn_b_fgate, L0_xattn_ln_weight, L0_ffn_w_router, L0_ffn_b_router, L0_ffn_we_gate,
           L0_ffn_we_up, L0_ffn_we_down, L0_ffn_ws_gate, L0_ffn_ws_up, L0_ffn_ws_down):
    import numpy as np
    import concourse.bacc as bacc
    from concourse.bass_utils import run_bass_kernel_spmd

    x = np.ascontiguousarray(x)
    E, D, F = L0_ffn_we_gate.shape
    P = 128
    w = np.concatenate([np.asarray(L0_xattn_w_igate), np.asarray(L0_xattn_w_fgate)], axis=0)
    w_gates = np.ascontiguousarray(w.T.reshape(-1, P, w.shape[0]).transpose(1, 0, 2))
    gu = np.stack([np.asarray(L0_ffn_we_gate).reshape(E, D // P, P, F),
                   np.asarray(L0_ffn_we_up).reshape(E, D // P, P, F)], axis=3)
    gu = gu.transpose(0, 2, 1, 3, 4).reshape(E, P, 2 * (D // P) * F)
    we = np.ascontiguousarray(np.concatenate([gu, np.asarray(L0_ffn_we_down)], axis=2))
    arrays = dict(
        x=x, ctx=ctx_1024, g_xattn=g_xattn, g_ffn=g_ffn, w_gates=w_gates,
        b_gates=np.concatenate([np.asarray(L0_xattn_b_igate), np.asarray(L0_xattn_b_fgate)]),
        ln_weight=L0_xattn_ln_weight, w_router=L0_ffn_w_router, b_router=L0_ffn_b_router, we=we,
        ws_gate=L0_ffn_ws_gate, ws_up=L0_ffn_ws_up, ws_down=L0_ffn_ws_down)
    nc = bacc.Bacc("TRN2", target_bir_lowering=False, num_devices=1)
    sent, args = {}, {}
    for name, a in arrays.items():
        a = np.ascontiguousarray(a)
        sent[f"in_{name}"] = a
        args[name] = nc.dram_tensor(f"in_{name}", a.shape, mybir.dt.from_np(a.dtype), kind="ExternalInput").ap()
    args["out"] = nc.dram_tensor("out_0", x.shape, mybir.dt.from_np(x.dtype), kind="ExternalOutput").ap()
    flamingo_moe(nc, **args)
    return run_bass_kernel_spmd(nc, [sent], core_ids=[0]).results[0]["out_0"]
```
